# Optimizing a Trainium2 kernel written in Bass

```python
import numpy as np
import jax
import jax.numpy as jnp

def _softmax(x, axis=-1):
    return jax.nn.softmax(x, axis=axis)

def _gelu(x):
    return jax.nn.gelu(x, approximate=True)

def _silu(x):
    return jax.nn.silu(x)

def _sigmoid(x):
    return jax.nn.sigmoid(x)

def _layernorm(x, axis=-1, eps=1e-05):
    m = jnp.mean(x, axis=axis, keepdims=True)
    v = jnp.var(x, axis=axis, keepdims=True)
    return (x - m) / jnp.sqrt(v + eps)

def _scatter_add(tgt, idx, src, axis=0):
    return tgt.at[idx].add(src)

def _segment_sum(src, seg, n):
    return jax.ops.segment_sum(src, seg, n)
kernel_name = 'mk_prb_d1_jaxref_r8_7d2ec1'

def setup_inputs(seed: int=0):
    np.random.seed(seed)
    _w = jnp.asarray

    def _L0_attn_setup():
        import jax, jax.numpy as jnp
        import numpy as np
        B, T, C = (2, 256, 256)
        N_HEAD, N_KV, HEAD_DIM = (32, 8, 64)
        REPEATS = N_HEAD // N_KV
        WINDOW = 128
        ROPE_BASE = 10000.0

        def _rope(q, k):
            D = q.shape[-1]
            inv_freq = 1.0 / ROPE_BASE ** (jnp.arange(0, D, 2, dtype=jnp.float32) / D)
            ang = jnp.arange(q.shape[2], dtype=jnp.float32)[:, None] * inv_freq[None, :]
            cos = jnp.concatenate([jnp.cos(ang), jnp.cos(ang)], axis=-1)
            sin = jnp.concatenate([jnp.sin(ang), jnp.sin(ang)], axis=-1)

            def rot_half(x):
                x1, x2 = jnp.split(x, 2, axis=-1)
                return jnp.concatenate([-x2, x1], axis=-1)

            def apply(x):
                return x * cos + rot_half(x) * sin
            return (apply(q), apply(k))
        key = jax.random.key(seed)
        ks = jax.random.split(key, 5)
        s = 0.02
        return {'x': jax.random.normal(ks[0], (B, T, C), jnp.float32), 'Wq': jax.random.normal(ks[1], (C, N_HEAD * HEAD_DIM), jnp.float32) * s, 'Wk': jax.random.normal(ks[2], (C, N_KV * HEAD_DIM), jnp.float32) * s, 'Wv': jax.random.normal(ks[3], (C, N_KV * HEAD_DIM), jnp.float32) * s, 'Wo': jax.random.normal(ks[4], (N_HEAD * HEAD_DIM, C), jnp.float32) * s}
    _L0_attn_in = _L0_attn_setup()

    def _L0_ffn_setup():
        import jax, jax.numpy as jnp
        import numpy as np
        HIDDEN = 256
        INTER = 1024
        SCALE = 64.0

        def fwht(x):
            orig_shape = x.shape
            n = orig_shape[-1]
            x = x.reshape(-1, n)
            h = 1
            while h < n:
                x = x.reshape(-1, n // (2 * h), 2, h)
                a, b = (x[:, :, 0, :], x[:, :, 1, :])
                x = jnp.stack([a + b, a - b], axis=2).reshape(-1, n)
                h *= 2
            return (x / jnp.sqrt(jnp.asarray(n, x.dtype))).reshape(orig_shape)
        key = jax.random.key(seed)
        ks = jax.random.split(key, 8)
        inp = jax.random.normal(ks[0], (4, 256, HIDDEN), dtype=jnp.float32)
        SU_ug = jnp.where(jax.random.bernoulli(ks[1], 0.5, (HIDDEN,)), 1.0, -1.0).astype(jnp.float32)
        SU_dp = jnp.where(jax.random.bernoulli(ks[2], 0.5, (INTER,)), 1.0, -1.0).astype(jnp.float32)
        Wscale_ug = jax.random.uniform(ks[3], (2 * INTER,), jnp.float32, 0.5, 1.5)
        Wscale_dp = jax.random.uniform(ks[4], (HIDDEN,), jnp.float32, 0.5, 1.5)
        W_up = jax.random.normal(ks[5], (INTER, HIDDEN), dtype=jnp.float32) * 0.02
        W_gate = jax.random.normal(ks[6], (INTER, HIDDEN), dtype=jnp.float32) * 0.02
        W_down = jax.random.normal(ks[7], (HIDDEN, INTER), dtype=jnp.float32) * 0.02
        return {'input': inp, 'SU_ug': SU_ug, 'SU_dp': SU_dp, 'Wscale_ug': Wscale_ug, 'Wscale_dp': Wscale_dp, 'W_up': W_up, 'W_gate': W_gate, 'W_down': W_down}
    _L0_ffn_in = _L0_ffn_setup()
    _d = {'L0_attn_x': _L0_attn_in['x'], 'L0_attn_Wq': _L0_attn_in['Wq'], 'L0_attn_Wk': _L0_attn_in['Wk'], 'L0_attn_Wv': _L0_attn_in['Wv'], 'L0_attn_Wo': _L0_attn_in['Wo'], 'L0_ffn_SU_ug': _L0_ffn_in['SU_ug'], 'L0_ffn_SU_dp': _L0_ffn_in['SU_dp'], 'L0_ffn_Wscale_ug': _L0_ffn_in['Wscale_ug'], 'L0_ffn_Wscale_dp': _L0_ffn_in['Wscale_dp'], 'L0_ffn_W_up': _L0_ffn_in['W_up'], 'L0_ffn_W_gate': _L0_ffn_in['W_gate'], 'L0_ffn_W_down': _L0_ffn_in['W_down']}
    _x0 = _d['L0_attn_x']
    _d['L0_attn_x'] = jax.random.normal(jax.random.fold_in(jax.random.key(seed), 1), (8, 512, 256), dtype=_x0.dtype)
    del _x0
    return _d

def reference(L0_attn_x, L0_attn_Wq, L0_attn_Wk, L0_attn_Wv, L0_attn_Wo, L0_ffn_SU_ug, L0_ffn_SU_dp, L0_ffn_Wscale_ug, L0_ffn_Wscale_dp, L0_ffn_W_up, L0_ffn_W_gate, L0_ffn_W_down):

    def _L0_attn_ref(x, Wq, Wk, Wv, Wo):
        import jax, jax.numpy as jnp
        import numpy as np
        B, T, C = (2, 256, 256)
        N_HEAD, N_KV, HEAD_DIM = (32, 8, 64)
        REPEATS = N_HEAD // N_KV
        WINDOW = 128
        ROPE_BASE = 10000.0

        def _rope(q, k):
            D = q.shape[-1]
            inv_freq = 1.0 / ROPE_BASE ** (jnp.arange(0, D, 2, dtype=jnp.float32) / D)
            ang = jnp.arange(q.shape[2], dtype=jnp.float32)[:, None] * inv_freq[None, :]
            cos = jnp.concatenate([jnp.cos(ang), jnp.cos(ang)], axis=-1)
            sin = jnp.concatenate([jnp.sin(ang), jnp.sin(ang)], axis=-1)

            def rot_half(x):
                x1, x2 = jnp.split(x, 2, axis=-1)
                return jnp.concatenate([-x2, x1], axis=-1)

            def apply(x):
                return x * cos + rot_half(x) * sin
            return (apply(q), apply(k))
        Bx, Tx, Cx = x.shape
        q = (x @ Wq).reshape(Bx, Tx, N_HEAD, HEAD_DIM).transpose(0, 2, 1, 3)
        k = (x @ Wk).reshape(Bx, Tx, N_KV, HEAD_DIM).transpose(0, 2, 1, 3)
        v = (x @ Wv).reshape(Bx, Tx, N_KV, HEAD_DIM).transpose(0, 2, 1, 3)
        q, k = _rope(q, k)
        qg = q.reshape(Bx, N_KV, REPEATS, Tx, HEAD_DIM)
        scale = 1.0 / jnp.sqrt(jnp.float32(HEAD_DIM))
        scores = jnp.einsum('bgrtd,bgsd->bgrts', qg, k) * scale
        i = jnp.arange(Tx)[:, None]
        j = jnp.arange(Tx)[None, :]
        allowed = (j <= i) & (i - j < WINDOW)
        scores = jnp.where(allowed, scores, -jnp.inf)
        attn = jax.nn.softmax(scores.astype(jnp.float32), axis=-1).astype(q.dtype)
        out = jnp.einsum('bgrts,bgsd->bgrtd', attn, v)
        out = out.reshape(Bx, N_HEAD, Tx, HEAD_DIM).transpose(0, 2, 1, 3).reshape(Bx, Tx, N_HEAD * HEAD_DIM)
        return out @ Wo

    def _L0_ffn_ref(input, SU_ug, SU_dp, Wscale_ug, Wscale_dp, W_up, W_gate, W_down):
        import jax, jax.numpy as jnp
        import numpy as np
        HIDDEN = 256
        INTER = 1024
        SCALE = 64.0

        def fwht(x):
            orig_shape = x.shape
            n = orig_shape[-1]
            x = x.reshape(-1, n)
            h = 1
            while h < n:
                x = x.reshape(-1, n // (2 * h), 2, h)
                a, b = (x[:, :, 0, :], x[:, :, 1, :])
                x = jnp.stack([a + b, a - b], axis=2).reshape(-1, n)
                h *= 2
            return (x / jnp.sqrt(jnp.asarray(n, x.dtype))).reshape(orig_shape)
        n = SU_ug.shape[0]
        x = input.reshape(-1, n)
        x = fwht(x * SU_ug) / SCALE
        x_up = x @ W_up.T * (Wscale_ug[:INTER] * SCALE)
        x_gate = x @ W_gate.T * (Wscale_ug[INTER:] * SCALE)
        x = jax.nn.silu(x_gate) * x_up
        x = fwht(x * SU_dp) / SCALE
        x = x @ W_down.T * (Wscale_dp * SCALE)
        return x.reshape(input.shape)
    x = L0_attn_x
    xn = _layernorm(x, axis=-1)
    x = x + _L0_attn_ref(xn, L0_attn_Wq, L0_attn_Wk, L0_attn_Wv, L0_attn_Wo) + _L0_ffn_ref(xn, L0_ffn_SU_ug, L0_ffn_SU_dp, L0_ffn_Wscale_ug, L0_ffn_Wscale_dp, L0_ffn_W_up, L0_ffn_W_gate, L0_ffn_W_down)
    return x

_drawn_inputs = setup_inputs


def setup_inputs(seed=0):
    import zlib

    import numpy as np

    out = dict(_drawn_inputs(seed))
    spreads = {}
    factors = {'L0_attn_Wq': 8.0, 'L0_attn_Wk': 8.0, 'L0_ffn_Wscale_ug': 3.958, 'L0_ffn_Wscale_dp': 5.499}
    for name, (base, spread) in spreads.items():
        noise = np.random.default_rng([zlib.crc32(name.encode()), seed]).standard_normal(out[name].shape)
        drawn = base * np.exp(spread * noise) if base else spread * noise
        out[name] = jnp.asarray(drawn.astype(out[name].dtype))
    for name, factor in factors.items():
        out[name] = (out[name] * factor).astype(out[name].dtype)
    return out
```

```python
import concourse.bass as bass
from concourse import mybir
from contextlib import ExitStack


def attention_and_ffn_block(
    nc: bass.Bass,
    x: bass.AP,
    wq: bass.AP,
    wk: bass.AP,
    wv: bass.AP,
    wo: bass.AP,
    su_in: bass.AP,
    su_mid: bass.AP,
    scale_gate_up: bass.AP,
    scale_down: bass.AP,
    w_gate_up: bass.AP,
    w_down: bass.AP,
    cos_k: bass.AP,
    sin_k: bass.AP,
    cos_q: bass.AP,
    sin_q: bass.AP,
    hadamard: bass.AP,
    identity: bass.AP,
    out: bass.AP,
):
    fp32 = mybir.dt.float32
    f32r = mybir.dt.float32r
    i8 = mybir.dt.int8
    ALU = mybir.AluOpType
    ACT = mybir.ActivationFunctionType
    AX = mybir.AxisListType

    P = 128
    BATCH, T, C = x.shape
    NH, NKV, D = 32, 8, 64
    HALF = D // 2
    REP = NH // NKV
    CT = C // P
    TT = T // P
    F = w_down.shape[0]
    FT = F // P
    STEPS = NKV * TT
    EPS = 1e-5
    MASKED = -3.0e38
    KV_PER_TILE = P // HALF
    SIDES = NKV // KV_PER_TILE

    ROPE_JOBS = [("k", 0), ("q", 0), ("q", 1), ("q", 2), ("q", 3), ("q", 4), ("k", 1), ("q", 5), ("q", 6), ("q", 7)]
    JOBS = len(ROPE_JOBS)
    K_STACKED = 4 * 16
    Q_STACKED = REP * 4 * 16

    def job(kind, n):
        return ROPE_JOBS.index((kind, n))

    def fillers(n):
        g, i = divmod(n, TT)
        found = []
        if g >= NKV:
            return found
        if i < 2 and g + 2 < NKV:
            found.append(("q", g + 2, i))
        if i >= 2 and g >= 1:
            found.append(("wo", g - 1, i - 2))
        if i >= 2 and g == KV_PER_TILE - 2:
            found.append(("k", 1, i - 2))
        return found

    USES = [("x", 0, 0), ("x", 0, 1), ("k", 0, 0), ("k", 0, 1)]
    USES += [("v", 0, i) for i in range(TT)]
    USES += [("q", 0, 0), ("q", 0, 1)]
    for j in range(2):
        USES += [("gate", j, 0), ("up", j, 0)]
    USES += [("q", 1, 0), ("q", 1, 1)]
    for j in range(2, FT):
        USES += [("gate", j, 0), ("up", j, 0)]
    for n in range(STEPS):
        USES += fillers(n)
    USES += [("wo", NKV - 1, 0), ("wo", NKV - 1, 1)]
    NUSES = len(USES)
    assert NUSES % 2 == 0 and len(set(USES)) == NUSES

    def use(*what):
        return USES.index(what)

    def masks_upto(n):
        return 2 * (n + 1) - (n // TT + 1)

    MASKS = masks_upto(STEPS - 1)

    def stacked(b, g, semaphores, each):
        return semaphores[g % 2], (b * (NKV // 2) + g // 2 + 1) * each

    ctx = ExitStack()
    with ctx:
        def sb(name, shape, dt=fp32):
            return ctx.enter_context(nc.sbuf_tensor(name, shape, dt))

        def sem(name):
            return ctx.enter_context(nc.semaphore(name))

        wq_p = [sb(f"wq_{s}", [P, CT, NH * D], f32r) for s in ("hi", "lo")]
        wk_p = [sb(f"wk_{s}", [P, CT, NKV * D], f32r) for s in ("hi", "lo")]
        wv_p = [sb(f"wv_{s}", [P, CT, NKV * D], f32r) for s in ("hi", "lo")]
        wgu_p = [sb(f"wgu_{s}", [P, CT, 2 * F], f32r) for s in ("hi", "lo")]
        wd_sb = sb("wd_sb", [P, FT, C])
        wo_sb = sb("wo_sb", [P, NH * D // P, C])
        tab = {k: sb(f"tab_{k}", [P, T]) for k in ("cos_k", "sin_k", "cos_q", "sin_q")}
        had = sb("had", [P, 2, P])
        ident = sb("ident", [P, P])
        later_key = sb("later_key", [P, REP, P], i8)
        masked = sb("masked", [P, 1])
        su_in_sb = sb("su_in_sb", [P, CT])
        su_mid_sb = sb("su_mid_sb", [P, FT])
        x_in = sb("x_in", [P, TT, C])
        acc = sb("acc", [P, TT, C])
        stats = sb("stats", [P, TT, 6])
        moments = sb("moments", [P, TT, 2])
        var_eps = sb("var_eps", [P, TT])
        std = sb("std", [P, TT])
        rstd = sb("rstd", [P, TT])
        xt_p = [sb(f"xt_{s}", [P, CT, T], f32r) for s in ("hi", "lo")]
        v_sb = sb("v_sb", [P, TT, NKV * D])
        prod = sb("prod", [P, 4, T])
        qy = sb("qy", [P, 2, 2, T], f32r)
        ky = sb("ky", [P, 2, 2, T], f32r)
        q_stack = sb("q_stack", [P, 2, REP, T], f32r)
        k_stack = sb("k_stack", [P, 2, 2, T], f32r)
        negmax = sb("negmax", [P, 2, REP])
        rowsum = sb("rowsum", [P, 2, REP])
        rinv = sb("rinv", [P, 2, REP])
        e_sb = sb("e_sb", [P, 2, REP, P])
        pt_sb = sb("pt_sb", [P, REP, P])
        p_cur = sb("p_cur", [P, 2, REP, P])
        p_prev = sb("p_prev", [P, 2, REP, P])
        o_t = sb("o_t", [P, REP // 2, T])
        xn = prod[:, 0:2, :].rearrange("p a (t c) -> p (a t) c", c=C)
        silu_sb = pt_sb[:, :, :].rearrange("p r q -> p (r q)")
        h_sb = [p_cur[:, n, :, :].rearrange("p r q -> p (r q)") for n in range(2)]
        stage = [prod[:, :, :].rearrange("p a t -> p (a t)"), v_sb[:, :, :].rearrange("p a t -> p (a t)")]
        scale_gu_b = [t[:, :, :, :].rearrange("p a r q -> p (a r q)") for t in (p_cur, p_prev)]
        folded = e_sb[:, :, :, :].rearrange("p a r q -> p a (r q)")
        scale_d_b = o_t[:, 0, 0:C]

        S = ctx.enter_context(nc.psum_tensor("S", [P, 2, 2, 2, 2 * P], fp32))
        TR = ctx.enter_context(nc.psum_tensor("TR", [P, REP, P], fp32))
        O = ctx.enter_context(nc.psum_tensor("O", [P, 512], fp32))
        PROJ = ctx.enter_context(nc.psum_tensor("PROJ", [P, 2, 512], fp32))
        S4 = S[:, :, :, :, :].rearrange("p a b h k -> p (a b) (h k)")

        def s_heads(n, which):
            return S[:, n % 2, :, :, which * P:(which + 1) * P].rearrange("p b h k -> p (b h) k")

        consts_in = sem("consts_in")
        w_in = [sem("w_in0"), sem("w_in1")]
        wo_in = sem("wo_in")
        scales_in = sem("scales_in")
        const_done = sem("const_done")
        w_hi = sem("w_hi")
        w_lo = sem("w_lo")
        su_done = sem("su_done")
        fold_ready = sem("fold_ready")
        fold_scaled = sem("fold_scaled")
        fold_hi = sem("fold_hi")
        fold_lo = sem("fold_lo")
        butterfly = sem("butterfly")
        wd_done = sem("wd_done")
        x_loaded = sem("x_loaded")
        stats_done = sem("stats_done")
        moments_done = sem("moments_done")
        var_done = sem("var_done")
        std_done = sem("std_done")
        rstd_done = sem("rstd_done")
        xn_done = sem("xn_done")
        acc_init = sem("acc_init")
        xt_hi_done = sem("xt_hi_done")
        xt_done = sem("xt_done")
        proj_ready = sem("proj_ready")
        v_done = sem("v_done")
        prod_done = sem("prod_done")
        rotated = sem("rotated")
        rope_hi = sem("rope_hi")
        rope_lo = sem("rope_lo")
        q_stacked = [sem("q_stacked0"), sem("q_stacked1")]
        k_stacked = [sem("k_stacked0"), sem("k_stacked1")]
        silu_done = sem("silu_done")
        h_done = sem("h_done")
        down_done = sem("down_done")
        ffn_added = sem("ffn_added")
        s_ready = sem("s_ready")
        s_folded = sem("s_folded")
        max_done = sem("max_done")
        exp_done = sem("exp_done")
        rinv_done = sem("rinv_done")
        norm_done = sem("norm_done")
        t_ready = sem("t_ready")
        t_copied = sem("t_copied")
        p_masked = sem("p_masked")
        pv_done = sem("pv_done")
        o_copied = sem("o_copied")
        wo_added = sem("wo_added")
        out_stored = sem("out_stored")

        waited = {e: sem(f"waited_{e}") for e in ("sp", "pool", "dve")}

        def wait_apart(eng, name, semaphore, value):
            eng.wait_ge(semaphore, value)
            eng.sem_inc(waited[name], 1)

        block = ctx.enter_context(nc.Block())

        CHUNKS = 6

        @block.sync
        def _(sp):
            def chunk(n, *parts):
                if n >= 2:
                    sp.wait_ge(w_lo, n - 1)
                for dst, src in parts:
                    sp.dma_start(dst, src).then_inc(w_in[n % 2], 16)

            tiles = lambda w: w.rearrange("(c p) n -> p c n", p=P)
            half = lambda n, a: stage[n][:, a * CT * NKV * D:(a + 1) * CT * NKV * D].rearrange("p (c n) -> p c n", c=CT)
            chunk(0, (half(0, 0), tiles(wk)), (half(0, 1), tiles(wv)))
            chunk(1, (stage[1], wq[0:P, :]))
            sp.dma_start(x_in[:, :, :], x[0, :, :].rearrange("(t p) c -> p t c", p=P)).then_inc(x_loaded, 16)
            chunk(2, (stage[0], wq[P:2 * P, :]))
            sp.wait_ge(w_lo, 2)
            sp.dma_start(stage[1], w_gate_up[0:P, :]).then_inc(w_in[1], 16)
            sp.wait_ge(w_lo, 3)
            sp.dma_start(stage[0], w_gate_up[P:2 * P, :]).then_inc(w_in[0], 16)
            sp.wait_ge(fold_ready, CT * 4)
            sp.dma_start(stage[0].rearrange("p (f c) -> p f c", f=FT),
                         w_down.rearrange("(f p) c -> p f c", p=P)).then_inc(w_in[0], 16)

            with sp.Fori(0, BATCH) as b:
                def stack_k(n):
                    side, j = divmod(n, KV_PER_TILE)
                    wait_apart(sp, "sp", rope_lo, b * JOBS + job("k", side) + 1)
                    if n >= 2:
                        wait_apart(sp, "sp", s_ready, b * STEPS + TT * (n - 1))
                    for quad in range(4):
                        sp.dma_start(k_stack[HALF * quad:HALF * (quad + 1), n % 2, :, :].bitcast(fp32),
                                     ky[HALF * j:HALF * (j + 1), quad % 2, :, :].bitcast(fp32)).then_inc(k_stacked[n % 2], 16)

                def stack_q(n):
                    wait_apart(sp, "sp", rope_lo, b * JOBS + job("q", n) + 1)
                    if n >= 2:
                        wait_apart(sp, "sp", s_ready, b * STEPS + TT * (n - 1))
                    for r in range(REP):
                        for quad in range(4):
                            sp.dma_start(q_stack[HALF * quad:HALF * (quad + 1), n % 2, r, :].bitcast(fp32),
                                         qy[HALF * r:HALF * (r + 1), quad % 2, quad // 2, :].bitcast(fp32)
                                         ).then_inc(q_stacked[n % 2], 16)

                stack_k(0)
                stack_k(1)
                stack_q(0)
                stack_q(1)
                wait_apart(sp, "sp", xn_done, b * TT + TT)
                wait_apart(sp, "sp", acc_init, b + 1)
                sp.dma_start(x_in[:, :, :],
                             x[bass.ds((b + 1) % BATCH, 1), :, :].rearrange("o (t p) c -> p (o t) c", p=P)
                             ).then_inc(x_loaded, 16)
                for n in range(2, NKV):
                    stack_q(n)
                    stack_k(n)
                wait_apart(sp, "sp", wo_added, (b + 1) * 2 * NKV + 2 * NKV)
                sp.dma_start(out[bass.ds(b, 1), :, :].rearrange("o (t p) c -> p (o t) c", p=P),
                             acc[:, :, :]).then_inc(out_stored, 16)
            sp.wait_ge(x_loaded, 16 * (BATCH + 1))
            sp.wait_ge(out_stored, 16 * (BATCH + 1))

        @block.gpsimd
        def _(pool):
            pool.sem_inc(out_stored, 16)
            nc.gpsimd.memset(masked[:, :], MASKED).then_inc(const_done, 1)
            nc.gpsimd.memset(later_key[:, :, :], 1).then_inc(const_done, 1)
            pool.wait_ge(const_done, 2)
            nc.gpsimd.affine_select(out=later_key[:, :, :], in_=later_key[:, :, :], compare_op=ALU.is_gt,
                                    fill=0.0, base=0, pattern=[[0, REP], [1, P]],
                                    channel_multiplier=-1).then_inc(const_done, 1)

            with pool.Fori(0, BATCH) as b:
                def rotate(kind, n):
                    j = job(kind, n)
                    pool.wait_ge(prod_done, b * 2 * JOBS + 2 * j + 2)
                    nc.gpsimd.tensor_tensor(prod[:, 0, :], prod[:, 0, :], prod[:, 2, :], ALU.subtract
                                            ).then_inc(rotated, 1)
                    nc.gpsimd.tensor_tensor(prod[:, 3, :], prod[:, 3, :], prod[:, 1, :], ALU.add
                                            ).then_inc(rotated, 1)

                def mask(n):
                    if n >= 2:
                        pool.wait_ge(pv_done, b * STEPS + n - 1)
                    wait_apart(pool, "pool", t_copied, b * STEPS + n + 1)
                    nc.gpsimd.affine_select(out=p_cur[:, n % 2, :, :], in_=pt_sb[:, :, :], compare_op=ALU.is_ge,
                                            fill=0.0, base=0, pattern=[[0, REP], [1, P]],
                                            channel_multiplier=-1).then_inc(p_masked, 1)
                    if n % TT:
                        nc.gpsimd.affine_select(out=p_prev[:, n % 2, :, :], in_=pt_sb[:, :, :],
                                                compare_op=ALU.is_gt, fill=0.0, base=0,
                                                pattern=[[0, REP], [-1, P]],
                                                channel_multiplier=1).then_inc(p_masked, 1)

                pool.wait_ge(x_loaded, b * 16 + 16)
                wait_apart(pool, "pool", out_stored, b * 16 + 16)
                nc.gpsimd.tensor_copy(acc[:, :, :], x_in[:, :, :]).then_inc(acc_init, 1)
                rotate("k", 0)
                rotate("q", 0)
                rotate("q", 1)
                for n in range(STEPS + 1):
                    for kind, m, part in fillers(n):
                        if kind in "qk" and part == 1:
                            rotate(kind, m)
                    if n >= 1:
                        mask(n - 1)

        @block.scalar
        def _(act):
            act.dma_start(ident[:, :], identity).then_inc(consts_in, 16)
            act.dma_start(had[:, :, :], hadamard.rearrange("s p n -> p s n")).then_inc(consts_in, 16)
            act.dma_start(su_in_sb[:, :], su_in).then_inc(consts_in, 16)
            act.dma_start(su_mid_sb[:, :], su_mid).then_inc(consts_in, 16)
            for k, src in (("cos_k", cos_k), ("sin_k", sin_k), ("cos_q", cos_q), ("sin_q", sin_q)):
                act.dma_start(tab[k][:, :], src).then_inc(consts_in, 16)
            for n in range(2):
                act.dma_start(scale_gu_b[n], scale_gate_up[n:n + 1, :].partition_broadcast(P)
                              ).then_inc(scales_in, 16)
            act.dma_start(scale_d_b, scale_down.partition_broadcast(P)).then_inc(scales_in, 16)
            act.dma_start(wo_sb[:, :, :], wo.rearrange("(m p) c -> p m c", p=P)).then_inc(wo_in, 16)

            act.wait_ge(w_in[0], 32)
            nc.scalar.activation(wk_p[0][:, :, :].rearrange("p c n -> p (c n)"), stage[0][:, 0:CT * NKV * D], ACT.Copy)
            nc.scalar.activation(wv_p[0][:, :, :].rearrange("p c n -> p (c n)"), stage[0][:, CT * NKV * D:], ACT.Copy
                                 ).then_inc(w_hi, 1)
            act.wait_ge(w_in[1], 16)
            nc.scalar.activation(wq_p[0][:, 0, :], stage[1], ACT.Copy).then_inc(w_hi, 1)
            act.wait_ge(w_in[0], 48)
            nc.scalar.activation(wq_p[0][:, 1, :], stage[0], ACT.Copy).then_inc(w_hi, 1)
            for n in range(CT * 4):
                c, k = divmod(n, 4)
                act.wait_ge(fold_scaled, n + 1)
                nc.scalar.activation(wgu_p[0][:, c, k * 512:(k + 1) * 512], folded[:, n % 2, :], ACT.Copy
                                     ).then_inc(fold_hi, 1)

            with act.Fori(0, BATCH) as b:
                def ready(*what):
                    act.wait_ge(proj_ready, b * NUSES + use(*what) + 1)

                def high(kind, n):
                    j = job(kind, n)
                    y = qy if kind == "q" else ky
                    act.wait_ge(rotated, b * 2 * JOBS + 2 * j + 2)
                    if kind == "q" and n >= 1:
                        act.wait_ge(*stacked(b, n - 1, q_stacked, Q_STACKED))
                    if kind == "k" and n >= 1:
                        for m in (2, 1):
                            act.wait_ge(*stacked(b, n * KV_PER_TILE - m, k_stacked, K_STACKED))
                    nc.scalar.activation(y[:, :, 0, :], prod[:, 0:4:3, :], ACT.Copy).then_inc(rope_hi, 1)

                def v_copy(i):
                    u = use("v", 0, i)
                    ready("v", 0, i)
                    nc.scalar.activation(v_sb[:, i, :], PROJ[:, u % 2, :], ACT.Copy).then_inc(v_done, 1)

                def silu(j):
                    u = use("gate", j, 0)
                    ready("gate", j, 0)
                    if j >= 1:
                        act.wait_ge(h_done, b * FT + j)
                    nc.scalar.activation(silu_sb, PROJ[:, u % 2, :], ACT.Silu
                                         ).then_inc(silu_done, 1)

                def exps(n):
                    act.wait_ge(max_done, b * STEPS + n + 1)
                    for r in range(REP):
                        last = nc.scalar.activation(e_sb[:, n % 2, r, :], s_heads(n, 1)[:, r, :], ACT.Exp,
                                                    bias=negmax[:, n % 2, r:r + 1],
                                                    accum_out=rowsum[:, n % 2, r:r + 1])
                    last.then_inc(exp_done, 1)

                def t_copy(n):
                    act.wait_ge(t_ready, b * STEPS + n + 1)
                    if n >= 1:
                        act.wait_ge(p_masked, b * MASKS + masks_upto(n - 1))
                    nc.scalar.activation(pt_sb[:, :, :], TR[:, :, :], ACT.Copy).then_inc(t_copied, 1)

                def o_copy(n):
                    i = n % TT
                    act.wait_ge(pv_done, b * STEPS + n + 1)
                    nc.scalar.activation(o_t[:, :, i * P:(i + 1) * P],
                                         O[:, 0:2 * P].rearrange("p (m q) -> p m q", m=2), ACT.Copy
                                         ).then_inc(o_copied, 1)

                act.wait_ge(var_done, b + 1)
                nc.scalar.activation(std[:, :], var_eps[:, :], ACT.Sqrt).then_inc(std_done, 1)
                for c in range(CT):
                    ready("x", 0, c)
                    nc.scalar.activation(xt_p[0][:, c, :], PROJ[:, c, :], ACT.Copy).then_inc(xt_hi_done, 1)
                v_copy(0)
                v_copy(1)
                high("k", 0)
                for i in range(2, TT):
                    v_copy(i)
                silu(0)
                high("q", 0)
                silu(1)
                silu(2)
                high("q", 1)
                for j in range(3, FT):
                    silu(j)

                for n in range(STEPS + 2):
                    if n < STEPS:
                        exps(n)
                    if n >= 2:
                        o_copy(n - 2)
                    for kind, m, part in fillers(n - 1):
                        if kind in "qk" and part == 1:
                            high(kind, m)
                    if 1 <= n <= STEPS:
                        t_copy(n - 1)

        @block.vector
        def _(dve):
            def low(dst, full, high):
                return nc.vector.tensor_tensor(dst, full, high.bitcast(fp32), ALU.subtract)

            dve.sem_inc(wo_added, 2 * NKV)
            dve.wait_ge(w_hi, 1)
            low(wk_p[1][:, :, :].rearrange("p c n -> p (c n)"), stage[0][:, 0:CT * NKV * D],
                wk_p[0][:, :, :].rearrange("p c n -> p (c n)"))
            low(wv_p[1][:, :, :].rearrange("p c n -> p (c n)"), stage[0][:, CT * NKV * D:],
                wv_p[0][:, :, :].rearrange("p c n -> p (c n)")).then_inc(w_lo, 1)
            dve.wait_ge(w_hi, 2)
            low(wq_p[1][:, 0, :], stage[1], wq_p[0][:, 0, :]).then_inc(w_lo, 1)
            dve.wait_ge(w_hi, 3)
            low(wq_p[1][:, 1, :], stage[0], wq_p[0][:, 1, :]).then_inc(w_lo, 1)
            dve.wait_ge(consts_in, 8 * 16)
            nc.vector.tensor_scalar(su_in_sb[:, :], su_in_sb[:, :], float(C) ** -0.5, None, ALU.mult).then_inc(su_done, 1)
            nc.vector.tensor_scalar(su_mid_sb[:, :], su_mid_sb[:, :], float(F) ** -0.5, None, ALU.mult).then_inc(su_done, 1)
            dve.wait_ge(su_done, 2)
            dve.wait_ge(scales_in, 3 * 16)
            for n in range(CT * 4):
                c, k = divmod(n, 4)
                dve.wait_ge(fold_ready, n + 1)
                if n >= 2:
                    dve.wait_ge(fold_lo, n - 1)
                nc.vector.scalar_tensor_tensor(
                    out=folded[:, n % 2, :], in0=PROJ[:, n % 2, :], scalar=su_in_sb[:, c:c + 1],
                    in1=scale_gu_b[k // 2][:, (k % 2) * 512:(k % 2 + 1) * 512],
                    op0=ALU.mult, op1=ALU.mult).then_inc(fold_scaled, 1)
                dve.wait_ge(fold_hi, n + 1)
                low(wgu_p[1][:, c, k * 512:(k + 1) * 512], folded[:, n % 2, :],
                    wgu_p[0][:, c, k * 512:(k + 1) * 512]).then_inc(fold_lo, 1)
            dve.wait_ge(w_in[0], 80)
            count = 0
            for level in range(3):
                src, dst = stage[level % 2], stage[(level + 1) % 2]
                h = 1 << level
                v_src = src.rearrange("p (a two h c) -> p a two (h c)", two=2, h=h, c=C)
                v_dst = dst.rearrange("p (a two h c) -> p a two (h c)", two=2, h=h, c=C)
                if count:
                    dve.wait_ge(butterfly, count)
                nc.vector.tensor_tensor(v_dst[:, :, 0, :], v_src[:, :, 0, :], v_src[:, :, 1, :], ALU.add
                                        ).then_inc(butterfly, 1)
                nc.vector.tensor_tensor(v_dst[:, :, 1, :], v_src[:, :, 0, :], v_src[:, :, 1, :], ALU.subtract
                                        ).then_inc(butterfly, 1)
                count += 2
            for n in range(FT // 2):
                dve.wait_ge(fold_ready, CT * 4 + n + 1)
                for k in range(2):
                    last = nc.vector.scalar_tensor_tensor(
                        out=wd_sb[:, 2 * n + k, :], in0=PROJ[:, n % 2, k * C:(k + 1) * C],
                        scalar=su_mid_sb[:, 2 * n + k:2 * n + k + 1], in1=scale_d_b, op0=ALU.mult, op1=ALU.mult)
                last.then_inc(wd_done, 1)

            with dve.Fori(0, BATCH) as b:
                def ready(*what):
                    dve.wait_ge(proj_ready, b * NUSES + use(*what) + 1)

                def products(kind, n, part):
                    j = job(kind, n)
                    u = use(kind, n, part)
                    cos, sin = tab["cos_" + kind], tab["sin_" + kind]
                    if part == 0 and j >= 1:
                        dve.wait_ge(rope_lo, b * JOBS + j)
                    ready(kind, n, part)
                    nc.vector.tensor_tensor(prod[:, 3 * part, :], PROJ[:, u % 2, :], cos[:, :], ALU.mult)
                    nc.vector.tensor_tensor(prod[:, 1 + part, :], PROJ[:, u % 2, :], sin[:, :], ALU.mult
                                            ).then_inc(prod_done, 1)

                def low_half(kind, n):
                    j = job(kind, n)
                    y = qy if kind == "q" else ky
                    dve.wait_ge(rope_hi, b * JOBS + j + 1)
                    low(y[:, :, 1, :], prod[:, 0:4:3, :], y[:, :, 0, :]).then_inc(rope_lo, 1)

                def hidden(j):
                    u = use("up", j, 0)
                    dve.wait_ge(silu_done, b * FT + j + 1)
                    ready("up", j, 0)
                    nc.vector.tensor_tensor(h_sb[j % 2], PROJ[:, u % 2, :], silu_sb, ALU.mult
                                            ).then_inc(h_done, 1)

                def wo_add(g, part):
                    u = use("wo", g, part)
                    k = 2 * g + part
                    ready("wo", g, part)
                    if k >= 2:
                        dve.wait_ge(wo_added, (b + 1) * 2 * NKV + k - 1)
                    a = acc[:, 2 * part:2 * part + 2, :]
                    nc.vector.tensor_tensor(a, PROJ[:, u % 2, :].rearrange("p (t c) -> p t c", t=2), a, ALU.add
                                            ).then_inc(wo_added, 1)

                def fold(n):
                    wait_apart(dve, "dve", s_ready, b * STEPS + n + 1)
                    own = s_heads(n, 1)
                    earlier = s_heads(n, 0) if n % TT else masked[:, :].rearrange("p (a k) -> p a k", a=1).to_broadcast([P, REP, P])
                    nc.vector.copy_predicated(own, later_key[:, :, :], earlier).then_inc(s_folded, 1)
                    dve.wait_ge(s_folded, b * STEPS + n + 1)
                    nc.vector.tensor_reduce(negmax[:, n % 2, :], own, axis=AX.X, op=ALU.max, negate=True
                                            ).then_inc(max_done, 1)

                def normalise(n):
                    dve.wait_ge(exp_done, b * STEPS + n + 1)
                    nc.vector.reciprocal(rinv[:, n % 2, :], rowsum[:, n % 2, :]).then_inc(rinv_done, 1)
                    dve.wait_ge(rinv_done, b * STEPS + n + 1)
                    e = e_sb[:, n % 2, :, :]
                    r = rinv[:, n % 2, :].rearrange("p (r o) -> p r o", o=1).to_broadcast([P, REP, P])
                    nc.vector.tensor_tensor(e, e, r, ALU.mult).then_inc(norm_done, 1)

                dve.wait_ge(x_loaded, b * 16 + 16)
                for t in range(TT):
                    last = nc.vector.bn_stats(stats[:, t, :], x_in[:, t, :])
                last.then_inc(stats_done, 1)
                wait_apart(dve, "dve", stats_done, b + 1)
                for t in range(TT):
                    last = nc.vector.bn_aggr(moments[:, t, :], stats[:, t, :])
                last.then_inc(moments_done, 1)
                dve.wait_ge(moments_done, b + 1)
                nc.vector.tensor_scalar(var_eps[:, :], moments[:, :, 1], EPS, None, ALU.add).then_inc(var_done, 1)
                dve.wait_ge(std_done, b + 1)
                nc.vector.reciprocal(rstd[:, :], std[:, :]).then_inc(rstd_done, 1)
                dve.wait_ge(rstd_done, b + 1)
                for t in range(TT):
                    nc.vector.tensor_scalar(xn[:, t, :], x_in[:, t, :], moments[:, t, 0:1], rstd[:, t:t + 1],
                                            ALU.subtract, ALU.mult).then_inc(xn_done, 1)
                for c in range(CT):
                    dve.wait_ge(xt_hi_done, b * CT + c + 1)
                    low(xt_p[1][:, c, :], PROJ[:, c, :], xt_p[0][:, c, :]
                        ).then_inc(xt_done, 1)
                products("k", 0, 0)
                products("k", 0, 1)
                low_half("k", 0)
                products("q", 0, 0)
                products("q", 0, 1)
                hidden(0)
                low_half("q", 0)
                hidden(1)
                products("q", 1, 0)
                products("q", 1, 1)
                hidden(2)
                low_half("q", 1)
                for j in range(3, FT):
                    hidden(j)
                dve.wait_ge(down_done, b + 1)
                dve.wait_ge(acc_init, b + 1)
                nc.vector.tensor_tensor(acc[:, :, :], S4[:, :, 0:C], acc[:, :, :], ALU.add).then_inc(ffn_added, 1)
                dve.wait_ge(ffn_added, b + 1)

                for n in range(STEPS):
                    fold(n)
                    for kind, m, part in fillers(n - 1):
                        if kind in "qk" and part == 1:
                            low_half(kind, m)
                    for kind, m, part in fillers(n):
                        if kind == "wo":
                            wo_add(m, part)
                        else:
                            products(kind, m, part)
                    normalise(n)
                wo_add(NKV - 1, 0)
                wo_add(NKV - 1, 1)

        @block.tensor
        def _(pe):
            def three(dst, lhs, rhs, first=True, last=True):
                nc.tensor.matmul(dst, lhs[0], rhs[0], start=first, stop=False)
                nc.tensor.matmul(dst, lhs[0], rhs[1], start=False, stop=False)
                return nc.tensor.matmul(dst, lhs[1], rhs[0], start=False, stop=last)

            pe.wait_ge(consts_in, 8 * 16)
            pe.wait_ge(w_in[1], 32)
            pe.wait_ge(w_in[0], 64)
            for n in range(CT * 4):
                c, k = divmod(n, 4)
                if n >= 2:
                    pe.wait_ge(fold_scaled, n - 1)
                for cc in range(CT):
                    last = nc.tensor.matmul(PROJ[:, n % 2, :], had[:, c * cc, :], stage[1 - cc][:, k * 512:(k + 1) * 512],
                                            start=cc == 0, stop=cc == CT - 1)
                last.then_inc(fold_ready, 1)
            pe.wait_ge(butterfly, 6)
            pe.wait_ge(fold_scaled, CT * 4)
            for n in range(FT // 2):
                if n >= 2:
                    pe.wait_ge(wd_done, n - 1)
                nc.tensor.matmul(PROJ[:, n % 2, :], had[:, 0, :], stage[1][:, n * 512:(n + 1) * 512],
                                 start=True, stop=True).then_inc(fold_ready, 1)
            pe.wait_ge(wd_done, FT // 2)
            pe.wait_ge(wo_in, 16)

            def has_read(b, u):
                what, n, part = USES[u]
                if u < 0:
                    assert what == "wo"
                    return wo_added, b * 2 * NKV + 2 * n + part + 1
                return {
                    "x": lambda: (xt_done, b * CT + part + 1),
                    "v": lambda: (v_done, b * TT + part + 1),
                    "k": lambda: (prod_done, b * 2 * JOBS + 2 * job("k", n) + part + 1),
                    "q": lambda: (prod_done, b * 2 * JOBS + 2 * job("q", n) + part + 1),
                    "gate": lambda: (silu_done, b * FT + n + 1),
                    "up": lambda: (h_done, b * FT + n + 1),
                    "wo": lambda: (wo_added, (b + 1) * 2 * NKV + 2 * n + part + 1),
                }[what]()

            with pe.Fori(0, BATCH) as b:
                def bank(*what):
                    u = use(*what)
                    pe.wait_ge(*has_read(b, u - 2))
                    return PROJ[:, u % 2, :]

                def project(kind, n, part):
                    w = wq_p if kind == "q" else wk_p
                    col = (2 * n + part) * P
                    dst = bank(kind, n, part)
                    for c in range(CT):
                        last = three(dst, [a[:, c, col:col + P] for a in w], [a[:, c, :] for a in xt_p],
                                     c == 0, c == CT - 1)
                    last.then_inc(proj_ready, 1)

                def values(i):
                    dst = bank("v", 0, i)
                    for c in range(CT):
                        last = three(dst, [a[:, c, i * P:(i + 1) * P] for a in xt_p], [a[:, c, :] for a in wv_p],
                                     c == 0, c == CT - 1)
                    last.then_inc(proj_ready, 1)

                def gate_up(j):
                    for k, name in enumerate(("gate", "up")):
                        col = (2 * j + k) * P
                        dst = bank(name, j, 0)
                        for c in range(CT):
                            last = three(dst, [a[:, c, col:col + P] for a in wgu_p], [a[:, c, :] for a in xt_p],
                                         c == 0, c == CT - 1)
                        last.then_inc(proj_ready, 1)

                def down(j):
                    pe.wait_ge(h_done, b * FT + j + 1)
                    for t in range(TT):
                        last = nc.tensor.matmul(S4[:, t, 0:C], h_sb[j % 2][:, t * P:(t + 1) * P], wd_sb[:, j, :],
                                                start=j == 0, stop=j == FT - 1)
                    if j == FT - 1:
                        last.then_inc(down_done, 1)

                def scores(n):
                    g, i = divmod(n, TT)
                    if i == 0:
                        pe.wait_ge(*stacked(b, g, q_stacked, Q_STACKED))
                        pe.wait_ge(*stacked(b, g, k_stacked, K_STACKED))
                    if n >= 2:
                        pe.wait_ge(exp_done, b * STEPS + n - 1)
                    k0, k1 = max(i - 1, 0) * P, (i + 1) * P
                    for r in range(REP):
                        dst = S[:, n % 2, r // 2, r % 2, 2 * P - (k1 - k0):2 * P]
                        q = q_stack[:, g % 2, r, i * P:(i + 1) * P]
                        nc.tensor.matmul(dst, q, k_stack[:, g % 2, 0, k0:k1], start=True, stop=False)
                        last = nc.tensor.matmul(dst, q, k_stack[:, g % 2, 1, k0:k1], start=False, stop=True)
                    last.then_inc(s_ready, 1)

                def transposes(n):
                    pe.wait_ge(norm_done, b * STEPS + n + 1)
                    if n >= 1:
                        pe.wait_ge(t_copied, b * STEPS + n)
                    for r in range(REP):
                        last = nc.tensor.transpose(TR[:, r, :], e_sb[:, n % 2, r, :], ident[:, :])
                    last.then_inc(t_ready, 1)

                def values_mixed(n):
                    g, i = divmod(n, TT)
                    pe.wait_ge(p_masked, b * MASKS + masks_upto(n))
                    if n == 0:
                        pe.wait_ge(v_done, b * TT + TT)
                    if n >= 1:
                        pe.wait_ge(o_copied, b * STEPS + n)
                    for odd in range(2):
                        dst = O[odd * D:(odd + 1) * D, 0:2 * P].rearrange("p (m q) -> p m q", m=2)
                        last = nc.tensor.matmul(dst, v_sb[:, i, g * D:(g + 1) * D], p_cur[:, n % 2, odd:REP:2, :],
                                         start=True, stop=i == 0)
                        if i:
                            last = nc.tensor.matmul(dst, v_sb[:, i - 1, g * D:(g + 1) * D],
                                                    p_prev[:, n % 2, odd:REP:2, :], start=False, stop=True)
                    last.then_inc(pv_done, 1)

                def project_out(g, part):
                    dst = bank("wo", g, part)
                    pe.wait_ge(o_copied, b * STEPS + TT * g + 2 * part + 2)
                    for t in range(2):
                        for m in range(2):
                            tok = (2 * part + t) * P
                            last = nc.tensor.matmul(dst[:, t * C:(t + 1) * C], o_t[:, m, tok:tok + P],
                                                    wo_sb[:, 2 * g + m, :], start=m == 0, stop=m == 1)
                    last.then_inc(proj_ready, 1)

                for c in range(CT):
                    dst = bank("x", 0, c)
                    for t in range(TT):
                        pe.wait_ge(xn_done, b * TT + t + 1)
                        last = nc.tensor.transpose(dst[:, t * P:(t + 1) * P], xn[:, t, c * P:(c + 1) * P], ident[:, :])
                    last.then_inc(proj_ready, 1)
                pe.wait_ge(xt_done, b * CT + CT)
                project("k", 0, 0)
                project("k", 0, 1)
                for i in range(TT):
                    values(i)
                project("q", 0, 0)
                project("q", 0, 1)
                gate_up(0)
                gate_up(1)
                down(0)
                project("q", 1, 0)
                project("q", 1, 1)
                down(1)
                for j in range(2, FT):
                    gate_up(j)
                    if j >= 3:
                        down(j - 1)
                down(FT - 1)
                pe.wait_ge(ffn_added, b + 1)
                for n in range(STEPS + 2):
                    if n < STEPS:
                        scores(n)
                    for kind, m, part in fillers(n):
                        (project_out if kind == "wo" else lambda *a, k=kind: project(k, *a))(m, part)
                    if n >= 2:
                        values_mixed(n - 2)
                    if 1 <= n <= STEPS:
                        transposes(n - 1)
                project_out(NKV - 1, 0)
                project_out(NKV - 1, 1)


def kernel(**inputs):
    import numpy as np
    import concourse.bacc as bacc
    from concourse.bass_utils import run_bass_kernel_spmd

    a = {k: np.asarray(v) for k, v in inputs.items()}
    NH, NKV, D, T = 32, 8, 64, 512
    C = a["L0_attn_x"].shape[2]
    F = a["L0_ffn_W_down"].shape[1]
    H, REP, FT = D // 2, NH // NKV, F // 128

    wq = a["L0_attn_Wq"].reshape(C, NKV, REP, 2, H).transpose(0, 1, 3, 2, 4).reshape(C, NH * D)
    wk = a["L0_attn_Wk"].reshape(C, NKV // 4, 4, 2, H).transpose(0, 1, 3, 2, 4).reshape(C, NKV * D)
    gate_up = np.stack([a["L0_ffn_W_gate"].reshape(FT, 128, C), a["L0_ffn_W_up"].reshape(FT, 128, C)], axis=1)
    gate_up = gate_up.reshape(2 * F, C).T
    s = a["L0_ffn_Wscale_ug"].reshape(2, FT, 128)
    scale_gate_up = np.stack([s[1], s[0]], axis=1).reshape(2, F)

    f4 = np.float32
    inv_freq = (f4(1.0) / f4(10000.0) ** (np.arange(0, D, 2, dtype=f4) / f4(D))).astype(f4)
    angle = (np.arange(T, dtype=f4)[:, None] * inv_freq[None, :]).astype(f4)
    cos = np.tile(np.cos(angle).astype(f4).T, (4, 1))
    sin = np.tile(np.sin(angle).astype(f4).T, (4, 1))
    had = np.ones((1, 1), f4)
    while had.shape[0] < 128:
        had = np.block([[had, had], [had, -had]])

    named = {
        "x": a["L0_attn_x"], "wq": wq, "wk": wk, "wv": a["L0_attn_Wv"], "wo": a["L0_attn_Wo"],
        "su_in": a["L0_ffn_SU_ug"].reshape(-1, 128).T, "su_mid": a["L0_ffn_SU_dp"].reshape(-1, 128).T, "scale_gate_up": scale_gate_up,
        "scale_down": a["L0_ffn_Wscale_dp"].reshape(1, C), "w_gate_up": gate_up, "w_down": a["L0_ffn_W_down"].T,
        "cos_k": cos, "sin_k": sin, "cos_q": cos * f4(D ** -0.5), "sin_q": sin * f4(D ** -0.5),
        "hadamard": np.stack([had, -had]), "identity": np.eye(128, dtype=f4),
    }
    nc = bacc.Bacc("TRN2", target_bir_lowering=False, num_devices=1)
    arrays, args = {}, []
    for name, v in named.items():
        v = np.ascontiguousarray(v)
        arrays[name] = v
        args.append(nc.dram_tensor(name, v.shape, mybir.dt.from_np(v.dtype), kind="ExternalInput").ap())
    shape = a["L0_attn_x"].shape
    args.append(nc.dram_tensor("out", shape, mybir.dt.float32, kind="ExternalOutput").ap())
    attention_and_ffn_block(nc, *args)
    r = run_bass_kernel_spmd(nc, [arrays], core_ids=[0])
    return r.results[0]["out"]
```

```python
import concourse.bass as bass
from concourse import mybir
from contextlib import ExitStack


def attention_and_ffn_block(
    nc: bass.Bass,
    x: bass.AP,
    wq: bass.AP,
    wk: bass.AP,
    wv: bass.AP,
    wo: bass.AP,
    su_in: bass.AP,
    su_mid: bass.AP,
    scale_gate_up: bass.AP,
    scale_down: bass.AP,
    w_gate_up: bass.AP,
    w_down: bass.AP,
    cos: bass.AP,
    sin: bass.AP,
    hadamard: bass.AP,
    identity: bass.AP,
    out: bass.AP,
):
    fp32 = mybir.dt.float32
    f32r = mybir.dt.float32r
    i8 = mybir.dt.int8
    ALU = mybir.AluOpType
    ACT = mybir.ActivationFunctionType
    AX = mybir.AxisListType

    P = 128
    BATCH, T, C = x.shape
    NH, NKV, D = 32, 8, 64
    HALF = D // 2
    REP = NH // NKV
    CT = C // P
    TT = T // P
    F = w_down.shape[0]
    FT = F // P
    STEPS = NKV * TT
    EPS = 1e-5
    MASKED = -3.0e38
    KV_PER_TILE = P // HALF
    SIDES = NKV // KV_PER_TILE

    ROPE_JOBS = [("k", 0), ("q", 0), ("q", 1), ("q", 2), ("q", 3), ("q", 4), ("k", 1), ("q", 5), ("q", 6), ("q", 7)]
    JOBS = len(ROPE_JOBS)
    K_STACKED = 4 * 16
    Q_STACKED = REP * 4 * 16

    def job(kind, n):
        return ROPE_JOBS.index((kind, n))

    NEXT = 1
    LAST_SLOT = STEPS + 2
    ROPE_SLOTS = {("q", 4, 0): (3, 4, 7, 8), ("k", 1, 0): (8, 9, 10, 11), ("q", 5, 0): (12, 13, 14, 15),
                  ("q", 6, 0): (16, 17, 18, 19), ("q", 7, 0): (20, 21, 22, 23), ("k", 0, NEXT): (28, 29, 30, 31)}
    NORM_SLOT = 24

    def rope_jobs(n, stage):
        return [what for what, slots in ROPE_SLOTS.items() if slots[stage] == n]

    def fillers(n):
        found = []
        if n < TT - 1:
            found.append(("v", 0, n + 1, 0))
        for part in range(2):
            found += [(kind, m, part, ahead) for kind, m, ahead in rope_jobs(n, part)]
        if n in (STEPS, STEPS + 1):
            found.append(("q", 0, n - STEPS, NEXT))
        if n >= TT + 2 and n % TT >= 2:
            found.append(("wo", n // TT - 1, n % TT - 2, 0))
        if n == NORM_SLOT + 1:
            found += [("x", 0, c, NEXT) for c in range(CT)]
        return found

    FIRST_USES = [("x", 0, 0, 0), ("x", 0, 1, 0), ("k", 0, 0, 0), ("k", 0, 1, 0), ("q", 0, 0, 0), ("q", 0, 1, 0)]
    USES = []
    HIDDEN_AFTER = {0: [0, 1], 1: [2, 3], 2: [4, 5], 3: [6, 7]}
    for n in range(4):
        for j in HIDDEN_AFTER[n]:
            if n and j == HIDDEN_AFTER[n][0]:
                USES += [("q", n, 0, 0), ("gate", j, 0, 0), ("q", n, 1, 0), ("up", j, 0, 0)]
            else:
                USES += [("gate", j, 0, 0), ("up", j, 0, 0)]
    USES.append(("v", 0, 0, 0))
    for n in range(LAST_SLOT + 1):
        USES += fillers(n)
    USES.append(("wo", NKV - 1, 1, 0))
    NUSES = len(USES)
    assert NUSES % 2 == 0 and len(set(USES)) == NUSES

    def place(turn, *what):
        if turn is None:
            u = FIRST_USES.index(what)
            return u % 2, u + 1
        u = USES.index(what)
        return u % 2, len(FIRST_USES) + turn * NUSES + u + 1

    def first(row):
        return type(row) is int

    def masks_upto(n):
        return 2 * (n + 1) - (n // TT + 1)

    MASKS = masks_upto(STEPS - 1)

    def stacked(b, g, semaphores, each):
        return semaphores[g % 2], (b * (NKV // 2) + g // 2 + 1) * each

    ctx = ExitStack()
    with ctx:
        def sb(name, shape, dt=fp32):
            return ctx.enter_context(nc.sbuf_tensor(name, shape, dt))

        def sem(name):
            return ctx.enter_context(nc.semaphore(name))

        wq_p = [sb(f"wq_{s}", [P, CT, NH * D], f32r) for s in ("hi", "lo")]
        wk_p = [sb(f"wk_{s}", [P, CT, NKV * D], f32r) for s in ("hi", "lo")]
        wv_p = [sb(f"wv_{s}", [P, CT, NKV * D], f32r) for s in ("hi", "lo")]
        wgu_p = [sb(f"wgu_{s}", [P, CT, 2 * F], f32r) for s in ("hi", "lo")]
        wd_sb = sb("wd_sb", [P, FT, C])
        wo_sb = sb("wo_sb", [P, NH * D // P, C])
        cos_sb = sb("cos_sb", [P, T])
        sin_sb = sb("sin_sb", [P, T])
        ident = sb("ident", [P, P])
        later_key = sb("later_key", [P, REP, P], i8)
        masked = sb("masked", [P, 1])
        su_in_sb = sb("su_in_sb", [P, CT])
        su_mid_sb = sb("su_mid_sb", [P, FT])
        x_in = sb("x_in", [P, TT, C])
        acc = sb("acc", [P, TT, C])
        stats = sb("stats", [P, TT, 6])
        moments = sb("moments", [P, TT, 2])
        spare = sb("spare", [P, 1])
        var_eps = sb("var_eps", [P, TT])
        std = sb("std", [P, TT])
        rstd = sb("rstd", [P, TT])
        xt_p = [sb(f"xt_{s}", [P, CT, T], f32r) for s in ("hi", "lo")]
        v_sb = sb("v_sb", [P, TT, NKV * D])
        prod = sb("prod", [P, 4, T])
        with ExitStack() as prologue:
            wq_stage = prologue.enter_context(nc.sbuf_tensor("wq_stage", [P, CT, NH * D], fp32))
            gu_stage = prologue.enter_context(nc.sbuf_tensor("gu_stage", [P, CT, 2 * F], fp32))
            down_stage = prologue.enter_context(nc.sbuf_tensor("down_stage", [P, FT * C], fp32))
        qy = sb("qy", [P, 2, 2, 2, T], f32r)
        q_stack = sb("q_stack", [P, 2, REP, T], f32r)
        k_stack = sb("k_stack", [P, 2, 2, T], f32r)
        ky = sb("ky", [P, 2, 2, T], f32r)
        negmax = sb("negmax", [P, 2, REP])
        rowsum = sb("rowsum", [P, 2, REP])
        rinv = sb("rinv", [P, 2, REP])
        e_sb = sb("e_sb", [P, 2, REP, P])
        pt_sb = sb("pt_sb", [P, REP, P])
        p_cur = sb("p_cur", [P, 2, REP, P])
        p_prev = sb("p_prev", [P, 2, REP, P])
        o_t = sb("o_t", [P, REP // 2, T])
        xn = prod[:, 0:2, :].rearrange("p a (t c) -> p (a t) c", c=C)
        silu_sb = pt_sb[:, :, :].rearrange("p r q -> p (r q)")
        h_sb = [p_cur[:, n, :, :].rearrange("p r q -> p (r q)") for n in range(2)]
        kv_stage = v_sb[:, :, :].rearrange("p a t -> p (a t)")
        wd_stage = [down_stage[:, :], kv_stage]
        scale_gu_b = [t[:, :, :, :].rearrange("p a r q -> p (a r q)") for t in (p_cur, p_prev)]
        folded = e_sb[:, :, :, :].rearrange("p a r q -> p a (r q)")
        scale_d_b = o_t[:, 0, 0:C]
        had = o_t[:, 1, 0:2 * P].rearrange("p (s n) -> p s n", s=2)

        S = ctx.enter_context(nc.psum_tensor("S", [P, 2, 2, 2, 2 * P], fp32))
        TR = ctx.enter_context(nc.psum_tensor("TR", [P, REP, P], fp32))
        O = ctx.enter_context(nc.psum_tensor("O", [P, 512], fp32))
        PROJ = ctx.enter_context(nc.psum_tensor("PROJ", [P, 2, 512], fp32))
        S4 = S[:, :, :, :, :].rearrange("p a b h k -> p (a b) (h k)")

        def s_heads(n, which):
            return S[:, n % 2, :, :, which * P:(which + 1) * P].rearrange("p b h k -> p (b h) k")

        consts_in = sem("consts_in")
        kv_in = sem("kv_in")
        wq_in = [sem("wq_in0"), sem("wq_in1")]
        gu_in = sem("gu_in")
        wd_in = sem("wd_in")
        wo_in = sem("wo_in")
        scales_in = sem("scales_in")
        const_done = sem("const_done")
        w_hi = sem("w_hi")
        w_lo = sem("w_lo")
        su_done = sem("su_done")
        fold_ready = sem("fold_ready")
        fold_scaled = sem("fold_scaled")
        fold_hi = sem("fold_hi")
        fold_lo = sem("fold_lo")
        butterfly = sem("butterfly")
        wd_done = sem("wd_done")
        x_loaded = sem("x_loaded")
        stats_done = sem("stats_done")
        moments_done = sem("moments_done")
        var_done = sem("var_done")
        std_done = sem("std_done")
        rstd_done = sem("rstd_done")
        xn_done = sem("xn_done")
        acc_init = sem("acc_init")
        xt_hi_done = sem("xt_hi_done")
        xt_done = sem("xt_done")
        proj_ready = sem("proj_ready")
        v_done = sem("v_done")
        prod_done = sem("prod_done")
        rotated = sem("rotated")
        rope_hi = sem("rope_hi")
        rope_lo = sem("rope_lo")
        q_stacked = [sem("q_stacked0"), sem("q_stacked1")]
        k_stacked = [sem("k_stacked0"), sem("k_stacked1")]
        silu_done = sem("silu_done")
        h_done = sem("h_done")
        down_done = sem("down_done")
        ffn_added = sem("ffn_added")
        s_ready = sem("s_ready")
        s_folded = sem("s_folded")
        max_done = sem("max_done")
        exp_done = sem("exp_done")
        rinv_done = sem("rinv_done")
        norm_done = sem("norm_done")
        t_ready = sem("t_ready")
        t_copied = sem("t_copied")
        p_masked = sem("p_masked")
        pv_done = sem("pv_done")
        o_copied = sem("o_copied")
        wo_added = sem("wo_added")
        out_stored = sem("out_stored")

        waited = {e: sem(f"waited_{e}") for e in ("sp", "pool", "dve")}

        def wait_apart(eng, name, semaphore, value):
            eng.wait_ge(semaphore, value)
            eng.sem_inc(waited[name], 1)

        block = ctx.enter_context(nc.Block())

        CONSTS = 6

        @block.sync
        def _(sp):
            tiles = lambda w: w.rearrange("(c p) n -> p c n", p=P)
            sp.dma_start(x_in[:, :, :], x[0, :, :].rearrange("(t p) c -> p t c", p=P)).then_inc(x_loaded, 16)
            for a, w in enumerate((wk, wv)):
                sp.dma_start(kv_stage[:, a * CT * NKV * D:(a + 1) * CT * NKV * D].rearrange("p (c n) -> p c n", c=CT),
                             tiles(w)).then_inc(kv_in, 16)
            sp.wait_ge(x_loaded, 16)
            sp.dma_start(gu_stage[:, 0, :], w_gate_up[0:P, :]).then_inc(gu_in, 16)
            sp.wait_ge(kv_in, 32)
            sp.dma_start(gu_stage[:, 1, :], w_gate_up[P:2 * P, :]).then_inc(gu_in, 16)
            sp.dma_start(wd_stage[0].rearrange("p (f c) -> p f c", f=FT),
                         w_down.rearrange("(f p) c -> p f c", p=P)).then_inc(wd_in, 16)
            for n in range(2):
                sp.dma_start(scale_gu_b[n], scale_gate_up[n:n + 1, :].partition_broadcast(P)
                              ).then_inc(scales_in, 16)
            sp.dma_start(scale_d_b, scale_down.partition_broadcast(P)).then_inc(scales_in, 16)
            sp.wait_ge(gu_in, CT * 16)
            for c in range(CT):
                sp.dma_start(wq_stage[:, c, :], wq[c * P:(c + 1) * P, :]).then_inc(wq_in[c], 16)
            sp.wait_ge(wq_in[0], 16)
            sp.dma_start(wo_sb[:, :, :], wo.rearrange("(m p) c -> p m c", p=P)).then_inc(wo_in, 16)
            sp.wait_ge(fold_ready, CT * 4)
            sp.wait_ge(butterfly, 6)

            with sp.Fori(0, BATCH) as b:
                def stack_k(n):
                    side, j = divmod(n, KV_PER_TILE)
                    wait_apart(sp, "sp", rope_lo, b * JOBS + job("k", side) + 1)
                    if n >= 2:
                        wait_apart(sp, "sp", s_ready, b * STEPS + TT * (n - 1))
                    for quad in range(4):
                        sp.dma_start(k_stack[HALF * quad:HALF * (quad + 1), n % 2, :, :].bitcast(fp32),
                                     ky[HALF * j:HALF * (j + 1), quad % 2, :, :].bitcast(fp32)).then_inc(k_stacked[n % 2], 16)

                def stack_q(n):
                    wait_apart(sp, "sp", rope_lo, b * JOBS + job("q", n) + 1)
                    if n >= 2:
                        wait_apart(sp, "sp", s_ready, b * STEPS + TT * (n - 1))
                    for r in range(REP):
                        for quad in range(4):
                            sp.dma_start(q_stack[HALF * quad:HALF * (quad + 1), n % 2, r, :].bitcast(fp32),
                                         qy[HALF * r:HALF * (r + 1), n % 2, quad % 2, quad // 2, :].bitcast(fp32)
                                         ).then_inc(q_stacked[n % 2], 16)

                stack_k(0)
                stack_q(0)
                wait_apart(sp, "sp", acc_init, b + 1)
                sp.dma_start(x_in[:, :, :],
                             x[bass.ds((b + 1) % BATCH, 1), :, :].rearrange("o (t p) c -> p (o t) c", p=P)
                             ).then_inc(x_loaded, 16)
                stack_q(1)
                stack_k(1)
                for n in range(2, NKV):
                    order = (stack_q, stack_k) if n == KV_PER_TILE else (stack_k, stack_q)
                    for stack in order:
                        stack(n)
                wait_apart(sp, "sp", wo_added, (b + 1) * 2 * NKV + 2 * NKV)
                sp.dma_start(out[bass.ds(b, 1), :, :].rearrange("o (t p) c -> p (o t) c", p=P),
                             acc[:, :, :]).then_inc(out_stored, 16)
            sp.wait_ge(x_loaded, 16 * (BATCH + 1))
            sp.wait_ge(out_stored, 16 * (BATCH + 1))

        @block.gpsimd
        def _(pool):
            pool.sem_inc(out_stored, 16)
            nc.gpsimd.memset(masked[:, :], MASKED).then_inc(const_done, 1)
            nc.gpsimd.memset(later_key[:, :, :], 1).then_inc(const_done, 1)
            pool.wait_ge(const_done, 2)
            nc.gpsimd.affine_select(out=later_key[:, :, :], in_=later_key[:, :, :], compare_op=ALU.is_gt,
                                    fill=0.0, base=0, pattern=[[0, REP], [1, P]],
                                    channel_multiplier=-1).then_inc(const_done, 1)

            def rotate(row, kind, n):
                pool.wait_ge(prod_done, row * 2 * JOBS + 2 * job(kind, n) + 2)
                nc.gpsimd.tensor_tensor(prod[:, 0, :], prod[:, 0, :], prod[:, 2, :], ALU.subtract
                                        ).then_inc(rotated, 1)
                nc.gpsimd.tensor_tensor(prod[:, 3, :], prod[:, 3, :], prod[:, 1, :], ALU.add
                                        ).then_inc(rotated, 1)

            rotate(0, "k", 0)
            pool.wait_ge(wd_in, 16)
            pool.wait_ge(w_lo, 1)
            for level in range(3):
                src, dst = wd_stage[level % 2], wd_stage[(level + 1) % 2]
                h = 1 << level
                v_src = src.rearrange("p (a two h c) -> p a two (h c)", two=2, h=h, c=C)
                v_dst = dst.rearrange("p (a two h c) -> p a two (h c)", two=2, h=h, c=C)
                if level:
                    pool.wait_ge(butterfly, 2 * level)
                nc.gpsimd.tensor_tensor(v_dst[:, :, 0, :], v_src[:, :, 0, :], v_src[:, :, 1, :], ALU.add
                                        ).then_inc(butterfly, 1)
                nc.gpsimd.tensor_tensor(v_dst[:, :, 1, :], v_src[:, :, 0, :], v_src[:, :, 1, :], ALU.subtract
                                        ).then_inc(butterfly, 1)
            with pool.Fori(0, BATCH) as b:
                def mask(n):
                    if n >= 2:
                        pool.wait_ge(pv_done, b * STEPS + n - 1)
                    wait_apart(pool, "pool", t_copied, b * STEPS + n + 1)
                    nc.gpsimd.affine_select(out=p_cur[:, n % 2, :, :], in_=pt_sb[:, :, :], compare_op=ALU.is_ge,
                                            fill=0.0, base=0, pattern=[[0, REP], [1, P]],
                                            channel_multiplier=-1).then_inc(p_masked, 1)
                    if n % TT:
                        nc.gpsimd.affine_select(out=p_prev[:, n % 2, :, :], in_=pt_sb[:, :, :],
                                                compare_op=ALU.is_gt, fill=0.0, base=0,
                                                pattern=[[0, REP], [-1, P]],
                                                channel_multiplier=1).then_inc(p_masked, 1)

                rotate(b, "q", 0)
                pool.wait_ge(x_loaded, b * 16 + 16)
                wait_apart(pool, "pool", out_stored, b * 16 + 16)
                nc.gpsimd.tensor_copy(acc[:, :, :], x_in[:, :, :]).then_inc(acc_init, 1)
                for n in range(1, 4):
                    rotate(b, "q", n)
                for n in range(STEPS + 2):
                    if n >= 2:
                        mask(n - 2)
                    for kind, m, ahead in rope_jobs(n, 1):
                        rotate(b + ahead, kind, m)

        @block.scalar
        def _(act):
            act.dma_start(ident[:, :], identity).then_inc(consts_in, 16)
            act.dma_start(had, hadamard.rearrange("s p n -> p s n")).then_inc(consts_in, 16)
            act.dma_start(su_in_sb[:, :], su_in).then_inc(consts_in, 16)
            act.dma_start(su_mid_sb[:, :], su_mid).then_inc(consts_in, 16)
            act.dma_start(cos_sb[:, :], cos).then_inc(consts_in, 16)
            act.dma_start(sin_sb[:, :], sin).then_inc(consts_in, 16)
            def deviation(row):
                act.wait_ge(var_done, row + 1)
                nc.scalar.activation(std[:, :], var_eps[:, :], ACT.Sqrt).then_inc(std_done, 1)

            def load_table(function):
                nc.scalar.activation(spare[:, :], ident[:, 0:1], function)

            def x_high(turn, ahead, c):
                bank, filled = place(turn, "x", 0, c, ahead)
                act.wait_ge(proj_ready, filled)
                nc.scalar.activation(xt_p[0][:, c, :], PROJ[:, bank, :], ACT.Copy).then_inc(xt_hi_done, 1)

            def high(row, kind, n):
                if kind == "q" and n >= 2:
                    act.wait_ge(*stacked(row, n - 2, q_stacked, Q_STACKED))
                if kind == "k" and (n or not first(row)):
                    prior, last = (row, KV_PER_TILE) if n else (row - 1, NKV)
                    for m in (2, 1):
                        act.wait_ge(*stacked(prior, last - m, k_stacked, K_STACKED))
                act.wait_ge(rotated, row * 2 * JOBS + 2 * job(kind, n) + 2)
                y = qy[:, n % 2, :, 0, :] if kind == "q" else ky[:, :, 0, :]
                nc.scalar.activation(y, prod[:, 0:4:3, :], ACT.Copy).then_inc(rope_hi, 1)

            deviation(0)
            act.wait_ge(kv_in, 32)
            nc.scalar.activation(wk_p[0][:, :, :].rearrange("p c n -> p (c n)"), kv_stage[:, 0:CT * NKV * D], ACT.Copy)
            nc.scalar.activation(wv_p[0][:, :, :].rearrange("p c n -> p (c n)"), kv_stage[:, CT * NKV * D:], ACT.Copy
                                 ).then_inc(w_hi, 1)
            x_high(None, 0, 0)
            x_high(None, 0, 1)
            for n in range(CT * 4):
                c, k = divmod(n, 4)
                act.wait_ge(fold_scaled, n + 1)
                nc.scalar.activation(wgu_p[0][:, c, k * 512:(k + 1) * 512], folded[:, n % 2, :], ACT.Copy
                                     ).then_inc(fold_hi, 1)
            for c in range(CT):
                act.wait_ge(wq_in[c], 16)
                nc.scalar.activation(wq_p[0][:, c, :], wq_stage[:, c, :], ACT.Copy, scale=D ** -0.5).then_inc(w_hi, 1)
            high(0, "k", 0)

            with act.Fori(0, BATCH) as b:
                def v_copy(i):
                    bank, filled = place(b, "v", 0, i, 0)
                    act.wait_ge(proj_ready, filled)
                    nc.scalar.activation(v_sb[:, i, :], PROJ[:, bank, :], ACT.Copy).then_inc(v_done, 1)

                def silu(j):
                    bank, filled = place(b, "gate", j, 0, 0)
                    act.wait_ge(proj_ready, filled)
                    if j >= 1:
                        act.wait_ge(h_done, b * FT + j)
                    nc.scalar.activation(silu_sb, PROJ[:, bank, :], ACT.Silu).then_inc(silu_done, 1)

                def exps(n):
                    act.wait_ge(max_done, b * STEPS + n + 1)
                    for r in range(REP):
                        last = nc.scalar.activation(e_sb[:, n % 2, r, :], s_heads(n, 1)[:, r, :], ACT.Exp,
                                                    bias=negmax[:, n % 2, r:r + 1],
                                                    accum_out=rowsum[:, n % 2, r:r + 1])
                    last.then_inc(exp_done, 1)

                def t_copy(n):
                    act.wait_ge(t_ready, b * STEPS + n + 1)
                    if n >= 1:
                        act.wait_ge(p_masked, b * MASKS + masks_upto(n - 1))
                    nc.scalar.activation(pt_sb[:, :, :], TR[:, :, :], ACT.Copy).then_inc(t_copied, 1)

                def o_copy(n):
                    i = n % TT
                    act.wait_ge(pv_done, b * STEPS + n + 1)
                    nc.scalar.activation(o_t[:, :, i * P:(i + 1) * P],
                                         O[:, 0:2 * P].rearrange("p (m q) -> p m q", m=2), ACT.Copy
                                         ).then_inc(o_copied, 1)

                silu(0)
                high(b, "q", 0)
                silu(1)
                for n in range(1, 4):
                    hidden = HIDDEN_AFTER[n]
                    if n == 3:
                        deviation(b + 1)
                    silu(hidden[0])
                    high(b, "q", n)
                    for j in hidden[1:]:
                        silu(j)
                load_table(ACT.Exp)
                v_copy(0)

                for n in range(LAST_SLOT + 1):
                    for kind, m, part, ahead in fillers(n):
                        if kind == "v":
                            v_copy(part)
                        elif kind == "x" and part == 0:
                            x_high(b, ahead, part)
                    if 2 <= n <= STEPS + 1:
                        t_copy(n - 2)
                    if n < STEPS:
                        exps(n)
                    if n == STEPS - 1:
                        load_table(ACT.Silu)
                    for kind, m, part, ahead in fillers(n):
                        if kind == "x" and part == 1:
                            x_high(b, ahead, part)
                    if n >= 3:
                        o_copy(n - 3)
                    for kind, m, ahead in rope_jobs(n, 2):
                        high(b + ahead, kind, m)

        @block.vector
        def _(dve):
            def low(dst, full, high):
                return nc.vector.tensor_tensor(dst, full, high.bitcast(fp32), ALU.subtract)

            def low_scaled(dst, full, high):
                return nc.vector.scalar_tensor_tensor(out=dst, in0=full, scalar=D ** -0.5, in1=high.bitcast(fp32),
                                                      op0=ALU.mult, op1=ALU.subtract)

            dve.sem_inc(wo_added, 2 * NKV)
            dve.wait_ge(consts_in, CONSTS * 16)
            def row_stats(row):
                dve.wait_ge(x_loaded, row * 16 + 16)
                for t in range(TT):
                    last = nc.vector.bn_stats(stats[:, t, :], x_in[:, t, :])
                last.then_inc(stats_done, 1)
                wait_apart(dve, "dve", stats_done, row + 1)
                for t in range(TT):
                    last = nc.vector.bn_aggr(moments[:, t, :], stats[:, t, :])
                last.then_inc(moments_done, 1)
                dve.wait_ge(moments_done, row + 1)
                nc.vector.tensor_scalar(var_eps[:, :], moments[:, :, 1], EPS, None, ALU.add).then_inc(var_done, 1)

            def row_rstd(row):
                dve.wait_ge(std_done, row + 1)
                nc.vector.reciprocal(rstd[:, :], std[:, :]).then_inc(rstd_done, 1)

            def row_normalised(row):
                dve.wait_ge(rstd_done, row + 1)
                for t in range(TT):
                    nc.vector.tensor_scalar(xn[:, t, :], x_in[:, t, :], moments[:, t, 0:1], rstd[:, t:t + 1],
                                            ALU.subtract, ALU.mult).then_inc(xn_done, 1)

            def x_low(turn, row, ahead, c):
                bank, _ = place(turn, "x", 0, c, ahead)
                dve.wait_ge(xt_hi_done, row * CT + c + 1)
                low(xt_p[1][:, c, :], PROJ[:, bank, :], xt_p[0][:, c, :]).then_inc(xt_done, 1)

            def products(turn, row, ahead, kind, n, part):
                j = job(kind, n)
                bank, filled = place(turn, kind, n, part, ahead)
                if part == 0 and (j or not first(row)):
                    dve.wait_ge(rope_lo, row * JOBS + j)
                dve.wait_ge(proj_ready, filled)
                nc.vector.tensor_tensor(prod[:, 3 * part, :], PROJ[:, bank, :], cos_sb[:, :], ALU.mult)
                nc.vector.tensor_tensor(prod[:, 1 + part, :], PROJ[:, bank, :], sin_sb[:, :], ALU.mult
                                        ).then_inc(prod_done, 1)

            def low_half(row, kind, n):
                y = qy[:, n % 2, :, :, :] if kind == "q" else ky[:, :, :, :]
                dve.wait_ge(rope_hi, row * JOBS + job(kind, n) + 1)
                low(y[:, :, 1, :], prod[:, 0:4:3, :], y[:, :, 0, :]).then_inc(rope_lo, 1)

            row_stats(0)
            row_rstd(0)
            row_normalised(0)
            dve.wait_ge(w_hi, 1)
            low(wk_p[1][:, :, :].rearrange("p c n -> p (c n)"), kv_stage[:, 0:CT * NKV * D],
                wk_p[0][:, :, :].rearrange("p c n -> p (c n)"))
            low(wv_p[1][:, :, :].rearrange("p c n -> p (c n)"), kv_stage[:, CT * NKV * D:],
                wv_p[0][:, :, :].rearrange("p c n -> p (c n)")).then_inc(w_lo, 1)
            for c in range(CT):
                x_low(None, 0, 0, c)
            products(None, 0, 0, "k", 0, 0)
            products(None, 0, 0, "k", 0, 1)
            nc.vector.tensor_scalar(su_in_sb[:, :], su_in_sb[:, :], float(C) ** -0.5, None, ALU.mult).then_inc(su_done, 1)
            nc.vector.tensor_scalar(su_mid_sb[:, :], su_mid_sb[:, :], float(F) ** -0.5, None, ALU.mult).then_inc(su_done, 1)
            dve.wait_ge(su_done, 2)
            dve.wait_ge(scales_in, 3 * 16)

            def fold_weights(n):
                c, k = divmod(n, 4)
                dve.wait_ge(fold_ready, n + 1)
                if n >= 2:
                    dve.wait_ge(fold_lo, n - 1)
                nc.vector.scalar_tensor_tensor(
                    out=folded[:, n % 2, :], in0=S4[:, n % 4, :], scalar=su_in_sb[:, c:c + 1],
                    in1=scale_gu_b[k // 2][:, (k % 2) * 512:(k % 2 + 1) * 512],
                    op0=ALU.mult, op1=ALU.mult).then_inc(fold_scaled, 1)

            fold_weights(0)
            for n in range(CT * 4):
                c, k = divmod(n, 4)
                if n + 1 < CT * 4:
                    fold_weights(n + 1)
                dve.wait_ge(fold_hi, n + 1)
                low(wgu_p[1][:, c, k * 512:(k + 1) * 512], folded[:, n % 2, :],
                    wgu_p[0][:, c, k * 512:(k + 1) * 512]).then_inc(fold_lo, 1)
            for c in range(CT):
                dve.wait_ge(w_hi, c + 2)
                low_scaled(wq_p[1][:, c, :], wq_stage[:, c, :], wq_p[0][:, c, :]).then_inc(w_lo, 1)
            low_half(0, "k", 0)
            products(None, 0, 0, "q", 0, 0)
            products(None, 0, 0, "q", 0, 1)
            for n in range(FT // 2):
                dve.wait_ge(fold_ready, CT * 4 + n + 1)
                for k in range(2):
                    last = nc.vector.scalar_tensor_tensor(
                        out=wd_sb[:, 2 * n + k, :], in0=S4[:, n, k * C:(k + 1) * C],
                        scalar=su_mid_sb[:, 2 * n + k:2 * n + k + 1], in1=scale_d_b, op0=ALU.mult, op1=ALU.mult)
                last.then_inc(wd_done, 1)

            with dve.Fori(0, BATCH) as b:
                def hidden(j):
                    bank, filled = place(b, "up", j, 0, 0)
                    dve.wait_ge(silu_done, b * FT + j + 1)
                    dve.wait_ge(proj_ready, filled)
                    nc.vector.tensor_tensor(h_sb[j % 2], PROJ[:, bank, :], silu_sb, ALU.mult).then_inc(h_done, 1)

                def wo_add(g, part):
                    bank, filled = place(b, "wo", g, part, 0)
                    k = 2 * g + part
                    dve.wait_ge(proj_ready, filled)
                    if k >= 2:
                        dve.wait_ge(wo_added, (b + 1) * 2 * NKV + k - 1)
                    a = acc[:, 2 * part:2 * part + 2, :]
                    nc.vector.tensor_tensor(a, PROJ[:, bank, :].rearrange("p (t c) -> p t c", t=2), a, ALU.add
                                            ).then_inc(wo_added, 1)

                def fold(n):
                    wait_apart(dve, "dve", s_ready, b * STEPS + n + 1)
                    own = s_heads(n, 1)
                    earlier = s_heads(n, 0) if n % TT else masked[:, :].rearrange("p (a k) -> p a k", a=1).to_broadcast([P, REP, P])
                    nc.vector.copy_predicated(own, later_key[:, :, :], earlier).then_inc(s_folded, 1)
                    dve.wait_ge(s_folded, b * STEPS + n + 1)
                    nc.vector.tensor_reduce(negmax[:, n % 2, :], own, axis=AX.X, op=ALU.max, negate=True
                                            ).then_inc(max_done, 1)

                def normalise(n):
                    dve.wait_ge(exp_done, b * STEPS + n + 1)
                    nc.vector.reciprocal(rinv[:, n % 2, :], rowsum[:, n % 2, :]).then_inc(rinv_done, 1)
                    dve.wait_ge(rinv_done, b * STEPS + n + 1)
                    e = e_sb[:, n % 2, :, :]
                    r = rinv[:, n % 2, :].rearrange("p (r o) -> p r o", o=1).to_broadcast([P, REP, P])
                    nc.vector.tensor_tensor(e, e, r, ALU.mult).then_inc(norm_done, 1)

                hidden(0)
                low_half(b, "q", 0)
                hidden(1)
                for n in range(1, 4):
                    products(b, b, 0, "q", n, 0)
                    products(b, b, 0, "q", n, 1)
                    js = HIDDEN_AFTER[n]
                    hidden(js[0])
                    if n == 2:
                        row_stats(b + 1)
                    low_half(b, "q", n)
                    for j in js[1:]:
                        hidden(j)
                dve.wait_ge(down_done, b + 1)
                dve.wait_ge(acc_init, b + 1)
                nc.vector.tensor_tensor(acc[:, :, :], S4[:, :, 0:C], acc[:, :, :], ALU.add).then_inc(ffn_added, 1)
                dve.wait_ge(ffn_added, b + 1)

                for n in range(LAST_SLOT + 1):
                    if n < STEPS:
                        fold(n)
                    if 1 <= n <= STEPS:
                        normalise(n - 1)
                    if n == 1:
                        row_rstd(b + 1)
                    for kind, m, ahead in rope_jobs(n, 3):
                        low_half(b + ahead, kind, m)
                    if n == NORM_SLOT:
                        dve.wait_ge(rope_lo, b * JOBS + JOBS)
                        row_normalised(b + 1)
                    for kind, m, part, ahead in fillers(n):
                        if kind == "wo":
                            wo_add(m, part)
                        elif kind == "x":
                            x_low(b, b + ahead, ahead, part)
                        elif kind != "v":
                            products(b, b + ahead, ahead, kind, m, part)
                wo_add(NKV - 1, 1)

        @block.tensor
        def _(pe):
            def three(dst, lhs, rhs, first=True, last=True):
                nc.tensor.matmul(dst, lhs[0], rhs[0], start=first, stop=False)
                nc.tensor.matmul(dst, lhs[0], rhs[1], start=False, stop=False)
                return nc.tensor.matmul(dst, lhs[1], rhs[0], start=False, stop=last)

            pe.wait_ge(consts_in, CONSTS * 16)

            def has_read(b, u):
                what, n, part, ahead = USES[u]
                turn = b - 1 if u < 0 else b
                row = turn + ahead
                if what == "wo":
                    return wo_added, (turn + 1) * 2 * NKV + 2 * n + part + 1
                if what == "x":
                    return xt_done, row * CT + part + 1
                if what == "v":
                    return v_done, row * TT + part + 1
                if what == "gate":
                    return silu_done, row * FT + n + 1
                if what == "up":
                    return h_done, row * FT + n + 1
                return prod_done, row * 2 * JOBS + 2 * job(what, n) + part + 1

            def bank(turn, *what):
                if turn is None:
                    u = FIRST_USES.index(what)
                    if u >= 4:
                        pe.wait_ge(prod_done, u - 3)
                    elif u >= 2:
                        pe.wait_ge(xt_done, u - 1)
                else:
                    u = USES.index(what)
                    pe.wait_ge(*has_read(turn, u - 2))
                return PROJ[:, u % 2, :]

            def transposed_x(turn, row, ahead, c):
                dst = bank(turn, "x", 0, c, ahead)
                for t in range(TT):
                    pe.wait_ge(xn_done, row * TT + t + 1)
                    last = nc.tensor.transpose(dst[:, t * P:(t + 1) * P], xn[:, t, c * P:(c + 1) * P], ident[:, :])
                last.then_inc(proj_ready, 1)

            def project(turn, row, ahead, kind, n, part):
                w = wq_p if kind == "q" else wk_p
                col = (2 * n + part) * P
                dst = bank(turn, kind, n, part, ahead)
                pe.wait_ge(xt_done, row * CT + CT)
                for c in range(CT):
                    last = three(dst, [a[:, c, col:col + P] for a in w], [a[:, c, :] for a in xt_p],
                                 c == 0, c == CT - 1)
                last.then_inc(proj_ready, 1)

            for c in range(CT):
                transposed_x(None, 0, 0, c)
            def first_heads(kind, parts_split):
                pe.wait_ge(w_lo, parts_split)
                for part in range(2):
                    project(None, 0, 0, kind, 0, part)

            first_heads("k", 1)
            pe.wait_ge(gu_in, CT * 16)
            for n in range(CT * 4):
                c, k = divmod(n, 4)
                if n >= 4:
                    pe.wait_ge(fold_scaled, n - 3)
                for cc in range(CT):
                    last = nc.tensor.matmul(S4[:, n % 4, :], had[:, c * cc, :], gu_stage[:, cc, k * 512:(k + 1) * 512],
                                            start=cc == 0, stop=cc == CT - 1)
                last.then_inc(fold_ready, 1)
            first_heads("q", 1 + CT)
            pe.wait_ge(butterfly, 6)
            for n in range(FT // 2):
                pe.wait_ge(fold_scaled, CT * 4 - 3 + n)
                nc.tensor.matmul(S4[:, n, :], had[:, 0, :], wd_stage[1][:, n * 512:(n + 1) * 512],
                                 start=True, stop=True).then_inc(fold_ready, 1)
            pe.wait_ge(fold_lo, CT * 4)
            pe.wait_ge(wd_done, FT // 2)
            pe.wait_ge(wo_in, 16)

            with pe.Fori(0, BATCH) as b:
                def values(i):
                    dst = bank(b, "v", 0, i, 0)
                    for c in range(CT):
                        last = three(dst, [a[:, c, i * P:(i + 1) * P] for a in xt_p], [a[:, c, :] for a in wv_p],
                                     c == 0, c == CT - 1)
                    last.then_inc(proj_ready, 1)

                def hidden(name, j):
                    col = (2 * j + (name == "up")) * P
                    dst = bank(b, name, j, 0, 0)
                    for c in range(CT):
                        last = three(dst, [a[:, c, col:col + P] for a in wgu_p], [a[:, c, :] for a in xt_p],
                                     c == 0, c == CT - 1)
                    last.then_inc(proj_ready, 1)

                def down(j):
                    pe.wait_ge(h_done, b * FT + j + 1)
                    for t in range(TT):
                        last = nc.tensor.matmul(S4[:, t, 0:C], h_sb[j % 2][:, t * P:(t + 1) * P], wd_sb[:, j, :],
                                                start=j == 0, stop=j == FT - 1)
                    if j == FT - 1:
                        last.then_inc(down_done, 1)

                def scores(n):
                    g, i = divmod(n, TT)
                    if i == 0:
                        pe.wait_ge(*stacked(b, g, q_stacked, Q_STACKED))
                        pe.wait_ge(*stacked(b, g, k_stacked, K_STACKED))
                    if n >= 2:
                        pe.wait_ge(exp_done, b * STEPS + n - 1)
                    k0, k1 = max(i - 1, 0) * P, (i + 1) * P
                    for r in range(REP):
                        dst = S[:, n % 2, r // 2, r % 2, 2 * P - (k1 - k0):2 * P]
                        q = q_stack[:, g % 2, r, i * P:(i + 1) * P]
                        nc.tensor.matmul(dst, q, k_stack[:, g % 2, 0, k0:k1], start=True, stop=False)
                        last = nc.tensor.matmul(dst, q, k_stack[:, g % 2, 1, k0:k1], start=False, stop=True)
                    last.then_inc(s_ready, 1)

                def transposes(n):
                    pe.wait_ge(norm_done, b * STEPS + n + 1)
                    if n >= 1:
                        pe.wait_ge(t_copied, b * STEPS + n)
                    for r in range(REP):
                        last = nc.tensor.transpose(TR[:, r, :], e_sb[:, n % 2, r, :], ident[:, :])
                    last.then_inc(t_ready, 1)

                def values_mixed(n):
                    g, i = divmod(n, TT)
                    pe.wait_ge(p_masked, b * MASKS + masks_upto(n) - (1 if i else 0))
                    if n < TT:
                        pe.wait_ge(v_done, b * TT + n + 1)
                    if n >= 1:
                        pe.wait_ge(o_copied, b * STEPS + n)
                    for earlier in range(2 if i else 1):
                        if earlier:
                            pe.wait_ge(p_masked, b * MASKS + masks_upto(n))
                        p = (p_cur, p_prev)[earlier]
                        for odd in range(2):
                            last = nc.tensor.matmul(O[odd * D:(odd + 1) * D, 0:2 * P].rearrange("p (m q) -> p m q", m=2),
                                                    v_sb[:, i - earlier, g * D:(g + 1) * D], p[:, n % 2, odd:REP:2, :],
                                                    start=earlier == 0, stop=i == 0 or earlier == 1)
                    last.then_inc(pv_done, 1)

                def project_out(g, part):
                    dst = bank(b, "wo", g, part, 0)
                    pe.wait_ge(o_copied, b * STEPS + TT * g + 2 * part + 2)
                    for t in range(2):
                        for m in range(2):
                            tok = (2 * part + t) * P
                            last = nc.tensor.matmul(dst[:, t * C:(t + 1) * C], o_t[:, m, tok:tok + P],
                                                    wo_sb[:, 2 * g + m, :], start=m == 0, stop=m == 1)
                    last.then_inc(proj_ready, 1)

                for n in range(4):
                    for j in HIDDEN_AFTER[n]:
                        alternate = n and j == HIDDEN_AFTER[n][0]
                        for part, name in enumerate(("gate", "up")):
                            if alternate:
                                project(b, b, 0, "q", n, part)
                            hidden(name, j)
                        if j:
                            down(j - 1)
                down(FT - 1)
                values(0)
                pe.wait_ge(ffn_added, b + 1)
                for n in range(LAST_SLOT + 1):
                    if n < STEPS:
                        scores(n)
                    if 2 <= n <= STEPS + 1:
                        transposes(n - 2)
                    for kind, m, part, ahead in fillers(n):
                        if kind == "wo":
                            project_out(m, part)
                        elif kind == "x":
                            transposed_x(b, b + ahead, ahead, part)
                        elif kind == "v":
                            values(part)
                        else:
                            project(b, b + ahead, ahead, kind, m, part)
                    if n >= 3:
                        values_mixed(n - 3)
                project_out(NKV - 1, 1)


def kernel(**inputs):
    import numpy as np
    import concourse.bacc as bacc
    from concourse.bass_utils import run_bass_kernel_spmd

    a = {k: np.asarray(v) for k, v in inputs.items()}
    NH, NKV, D, T = 32, 8, 64, 512
    C = a["L0_attn_x"].shape[2]
    F = a["L0_ffn_W_down"].shape[1]
    H, REP, FT = D // 2, NH // NKV, F // 128

    wq = a["L0_attn_Wq"].reshape(C, NKV, REP, 2, H).transpose(0, 1, 3, 2, 4).reshape(C, NH * D)
    wk = a["L0_attn_Wk"].reshape(C, NKV // 4, 4, 2, H).transpose(0, 1, 3, 2, 4).reshape(C, NKV * D)
    gate_up = np.stack([a["L0_ffn_W_gate"].reshape(FT, 128, C), a["L0_ffn_W_up"].reshape(FT, 128, C)], axis=1)
    gate_up = gate_up.reshape(2 * F, C).T
    s = a["L0_ffn_Wscale_ug"].reshape(2, FT, 128)
    scale_gate_up = np.stack([s[1], s[0]], axis=1).reshape(2, F)

    f4 = np.float32
    inv_freq = (f4(1.0) / f4(10000.0) ** (np.arange(0, D, 2, dtype=f4) / f4(D))).astype(f4)
    angle = (np.arange(T, dtype=f4)[:, None] * inv_freq[None, :]).astype(f4)
    cos = np.tile(np.cos(angle).astype(f4).T, (4, 1))
    sin = np.tile(np.sin(angle).astype(f4).T, (4, 1))
    had = np.ones((1, 1), f4)
    while had.shape[0] < 128:
        had = np.block([[had, had], [had, -had]])

    named = {
        "x": a["L0_attn_x"], "wq": wq, "wk": wk, "wv": a["L0_attn_Wv"], "wo": a["L0_attn_Wo"],
        "su_in": a["L0_ffn_SU_ug"].reshape(-1, 128).T, "su_mid": a["L0_ffn_SU_dp"].reshape(-1, 128).T, "scale_gate_up": scale_gate_up,
        "scale_down": a["L0_ffn_Wscale_dp"].reshape(1, C), "w_gate_up": gate_up, "w_down": a["L0_ffn_W_down"].T,
        "cos": cos, "sin": sin,
        "hadamard": np.stack([had, -had]), "identity": np.eye(128, dtype=f4),
    }
    nc = bacc.Bacc("TRN2", target_bir_lowering=False, num_devices=1)
    arrays, args = {}, []
    for name, v in named.items():
        v = np.ascontiguousarray(v)
        arrays[name] = v
        args.append(nc.dram_tensor(name, v.shape, mybir.dt.from_np(v.dtype), kind="ExternalInput").ap())
    shape = a["L0_attn_x"].shape
    args.append(nc.dram_tensor("out", shape, mybir.dt.float32, kind="ExternalOutput").ap())
    attention_and_ffn_block(nc, *args)
    r = run_bass_kernel_spmd(nc, [arrays], core_ids=[0])
    return r.results[0]["out"]
```
